# Optimizing a Trainium2 kernel written in Bass

```python
import numpy as np
import jax
import jax.numpy as jnp

def _softmax(x, axis=-1):
    return jax.nn.softmax(x, axis=axis)

def _gelu(x):
    return jax.nn.gelu(x, approximate=True)

def _silu(x):
    return jax.nn.silu(x)

def _sigmoid(x):
    return jax.nn.sigmoid(x)

def _layernorm(x, axis=-1, eps=1e-05):
    m = jnp.mean(x, axis=axis, keepdims=True)
    v = jnp.var(x, axis=axis, keepdims=True)
    return (x - m) / jnp.sqrt(v + eps)

def _scatter_add(tgt, idx, src, axis=0):
    return tgt.at[idx].add(src)

def _segment_sum(src, seg, n):
    return jax.ops.segment_sum(src, seg, n)
kernel_name = 'mk_adj_preln_d4_adj_r2_318d94'

def setup_inputs(seed: int=0):
    np.random.seed(seed)
    _w = jnp.asarray

    def _rec_inputs():
        import jax
        import jax.numpy as jnp
        _gk = jax.random.key(seed)
        x = -0.000929 + 1 * jax.random.normal(jax.random.fold_in(_gk, 1), (2048, 128), jnp.float32)
        _a = jax.random.bernoulli(jax.random.fold_in(_gk, 2), 0.0078125, (2048, 2048))
        _a = jnp.logical_or(_a, jnp.eye(2048, dtype=bool))
        _af = _a.astype(jnp.float32)
        _af = _af * jax.random.uniform(jax.random.fold_in(_gk, 3), (2048, 2048), jnp.float32, 0.05, 1)
        adj = _af
        return (x, adj)
    x, adj = _rec_inputs()

    def _L0_gnn_setup():
        import jax, jax.numpy as jnp
        import numpy as np
        N, E, D = (4096, 4096, 128)
        key = jax.random.key(seed)
        k1, k2 = jax.random.split(key)
        X = jax.random.normal(k1, (N, D), dtype=jnp.float32)
        H = jax.random.uniform(k2, (N, E), dtype=jnp.float32)
        return {'X': X, 'H': H}
    _L0_gnn_all = _L0_gnn_setup()
    _L0_gnn_in = {k: v for k, v in _L0_gnn_all.items() if k in ()}
    del _L0_gnn_all

    def _L1_gnn_setup():
        import jax, jax.numpy as jnp
        import numpy as np
        IN_DIM = 128
        OUT_DIM = 128
        N = 8192
        key = jax.random.key(seed)
        k_x, k_adj, k_w, k_b = jax.random.split(key, 4)
        x = jax.random.normal(k_x, (N, IN_DIM), dtype=jnp.float32)
        adj = jax.random.uniform(k_adj, (N, N), dtype=jnp.float32)
        bound = 1.0 / np.sqrt(2 * IN_DIM)
        W = jax.random.uniform(k_w, (OUT_DIM, 2 * IN_DIM), dtype=jnp.float32, minval=-bound, maxval=bound)
        b = jax.random.uniform(k_b, (OUT_DIM,), dtype=jnp.float32, minval=-bound, maxval=bound)
        return {'x': x, 'adj': adj, 'W': W, 'b': b}
    _L1_gnn_all = _L1_gnn_setup()
    _L1_gnn_in = {k: v for k, v in _L1_gnn_all.items() if k in ('W', 'b')}
    del _L1_gnn_all

    def _L2_gnn_setup():
        import jax, jax.numpy as jnp
        import numpy as np
        N0 = 2048
        C = 128
        DEPTH = 3
        RATIO = 0.5
        AVG_DEG = 32
        BN_EPS = 1e-05

        def _gcn(x, A, W, b):
            n = A.shape[0]
            Ah = A + 2.0 * jnp.eye(n, dtype=A.dtype)
            deg = Ah.sum(axis=1)
            d_safe = jnp.where(deg > 0, deg, 1.0)
            dn = jnp.where(deg > 0, jax.lax.rsqrt(d_safe), 0.0)
            An = dn[:, None] * Ah * dn[None, :]
            return An @ (x @ W) + b

        def _bn(x, g, b):
            m = x.mean(axis=0)
            v = x.var(axis=0)
            return g * (x - m) * jax.lax.rsqrt(v + BN_EPS) + b

        def _augment(A):
            n = A.shape[0]
            I = jnp.eye(n, dtype=A.dtype)
            Aa = A + I
            return Aa @ Aa * (1.0 - I)

        def _topk_pool(x, A, p):
            score = jnp.tanh(x @ p / jnp.linalg.norm(p))
            k = int(np.ceil(RATIO * x.shape[0]))
            vals, perm = jax.lax.top_k(score, k)
            xn = x[perm] * vals[:, None]
            An = A[perm][:, perm]
            return (xn, An, perm)
        key = jax.random.key(seed)
        ks = jax.random.split(key, 6)
        x = jax.random.normal(ks[0], (N0, C), dtype=jnp.float32)
        mask = jax.random.bernoulli(ks[1], AVG_DEG / N0, (N0, N0)).astype(jnp.float32)
        adj = jnp.maximum(mask, mask.T) * (1.0 - jnp.eye(N0, dtype=jnp.float32))
        scale = 1.0 / np.sqrt(C)
        conv_w = jax.random.normal(ks[2], (2 * DEPTH + 1, C, C), dtype=jnp.float32) * scale
        conv_b = jax.random.normal(ks[3], (2 * DEPTH + 1, C), dtype=jnp.float32) * 0.01
        pool_w = jax.random.normal(ks[4], (DEPTH, C), dtype=jnp.float32)
        bn_g = jnp.ones((2 * DEPTH + 1, C), dtype=jnp.float32)
        bn_b = jnp.zeros((2 * DEPTH + 1, C), dtype=jnp.float32)
        return {'x': x, 'adj': adj, 'conv_w': conv_w, 'conv_b': conv_b, 'pool_w': pool_w, 'bn_g': bn_g, 'bn_b': bn_b}
    _L2_gnn_all = _L2_gnn_setup()
    _L2_gnn_in = {k: v for k, v in _L2_gnn_all.items() if k in ('conv_w', 'conv_b', 'pool_w', 'bn_g', 'bn_b')}
    del _L2_gnn_all

    def _L3_gnn_setup():
        import jax, jax.numpy as jnp
        import numpy as np
        N = 8192
        F_IN = 128
        F_OUT = 128
        key = jax.random.key(seed)
        k1, k2, k3 = jax.random.split(key, 3)
        x = jax.random.normal(k1, (N, F_IN), dtype=jnp.float32)
        adj = jax.random.uniform(k2, (N, N), dtype=jnp.float32)
        stdv = 1.0 / np.sqrt(F_OUT)
        w = jax.random.uniform(k3, (2 * F_IN, F_OUT), dtype=jnp.float32, minval=-stdv, maxval=stdv)
        return {'input': x, 'adj': adj, 'weight': w}
    _L3_gnn_all = _L3_gnn_setup()
    _L3_gnn_in = {k: v for k, v in _L3_gnn_all.items() if k in ('weight',)}
    del _L3_gnn_all
    return {'x': x, 'adj': adj, 'L1_gnn_W': _L1_gnn_in['W'], 'L1_gnn_b': _L1_gnn_in['b'], 'L2_gnn_conv_w': _L2_gnn_in['conv_w'], 'L2_gnn_conv_b': _L2_gnn_in['conv_b'], 'L2_gnn_pool_w': _L2_gnn_in['pool_w'], 'L2_gnn_bn_g': _L2_gnn_in['bn_g'], 'L2_gnn_bn_b': _L2_gnn_in['bn_b'], 'L3_gnn_weight': _L3_gnn_in['weight']}

def reference(x, adj, L1_gnn_W, L1_gnn_b, L2_gnn_conv_w, L2_gnn_conv_b, L2_gnn_pool_w, L2_gnn_bn_g, L2_gnn_bn_b, L3_gnn_weight):
    import jax
    import jax.numpy as jnp

    def _L0_gnn_ref(X, H):
        import jax, jax.numpy as jnp
        import numpy as np
        N, E, D = (4096, 4096, 128)
        msg = jnp.matmul(H.T, X)
        inv_deg = 1.0 / H.sum(axis=0)
        inv_deg = jnp.where(jnp.isinf(inv_deg), 0.0, inv_deg)
        return msg * inv_deg[:, None]

    def _L1_gnn_ref(x, adj, W, b):
        import jax, jax.numpy as jnp
        import numpy as np
        IN_DIM = 128
        OUT_DIM = 128
        N = 8192
        h_N = jnp.matmul(adj, x)
        h_cat = jnp.concatenate([x, h_N], axis=-1)
        out = jnp.maximum(jnp.einsum('nd,od->no', h_cat, W) + b, 0.0)
        return out

    def _L2_gnn_ref(x, adj, conv_w, conv_b, pool_w, bn_g, bn_b):
        import jax, jax.numpy as jnp
        import numpy as np
        N0 = 2048
        C = 128
        DEPTH = 3
        RATIO = 0.5
        AVG_DEG = 32
        BN_EPS = 1e-05

        def _gcn(x, A, W, b):
            n = A.shape[0]
            Ah = A + 2.0 * jnp.eye(n, dtype=A.dtype)
            deg = Ah.sum(axis=1)
            d_safe = jnp.where(deg > 0, deg, 1.0)
            dn = jnp.where(deg > 0, jax.lax.rsqrt(d_safe), 0.0)
            An = dn[:, None] * Ah * dn[None, :]
            return An @ (x @ W) + b

        def _bn(x, g, b):
            m = x.mean(axis=0)
            v = x.var(axis=0)
            return g * (x - m) * jax.lax.rsqrt(v + BN_EPS) + b

        def _augment(A):
            n = A.shape[0]
            I = jnp.eye(n, dtype=A.dtype)
            Aa = A + I
            return Aa @ Aa * (1.0 - I)

        def _topk_pool(x, A, p):
            score = jnp.tanh(x @ p / jnp.linalg.norm(p))
            k = int(np.ceil(RATIO * x.shape[0]))
            vals, perm = jax.lax.top_k(score, k)
            xn = x[perm] * vals[:, None]
            An = A[perm][:, perm]
            return (xn, An, perm)
        x = x.astype(jnp.float32)
        x = _bn(jax.nn.relu(_gcn(x, adj, conv_w[0], conv_b[0])), bn_g[0], bn_b[0])
        xs, adjs, perms = ([x], [adj], [])
        A = adj
        for i in range(1, DEPTH + 1):
            A2 = _augment(A)
            x, A, perm = _topk_pool(x, A2, pool_w[i - 1])
            x = _bn(jax.nn.relu(_gcn(x, A, conv_w[i], conv_b[i])), bn_g[i], bn_b[i])
            if i < DEPTH:
                xs.append(x)
                adjs.append(A)
            perms.append(perm)
        for i in range(DEPTH):
            j = DEPTH - 1 - i
            res, Aj, perm = (xs[j], adjs[j], perms[j])
            up = jnp.zeros_like(res).at[perm].set(x)
            x = res + up
            x = _gcn(x, Aj, conv_w[DEPTH + 1 + i], conv_b[DEPTH + 1 + i])
            if i < DEPTH - 1:
                x = jax.nn.relu(x)
            x = _bn(x, bn_g[DEPTH + 1 + i], bn_b[DEPTH + 1 + i])
        return x

    def _L3_gnn_ref(input, adj, weight):
        import jax, jax.numpy as jnp
        import numpy as np
        N = 8192
        F_IN = 128
        F_OUT = 128
        support = adj @ input
        h = jnp.concatenate([input, support], axis=1)
        return h @ weight
    h = jnp.maximum(_layernorm(x, axis=-1), 0.0)
    x = x + _L0_gnn_ref(h, adj)
    h = jnp.maximum(_layernorm(x, axis=-1), 0.0)
    x = x + _L1_gnn_ref(h, adj, L1_gnn_W, L1_gnn_b)
    h = jnp.maximum(_layernorm(x, axis=-1), 0.0)
    x = x + _L2_gnn_ref(h, adj, L2_gnn_conv_w, L2_gnn_conv_b, L2_gnn_pool_w, L2_gnn_bn_g, L2_gnn_bn_b)
    h = jnp.maximum(_layernorm(x, axis=-1), 0.0)
    x = x + _L3_gnn_ref(h, adj, L3_gnn_weight)
    return x

_drawn_inputs = setup_inputs


def setup_inputs(seed=0):
    import zlib

    import numpy as np

    out = dict(_drawn_inputs(seed))
    spreads = {'L2_gnn_bn_g': (1.0, 0.2), 'L2_gnn_bn_b': (0.0, 0.1)}
    factors = {}
    for name, (base, spread) in spreads.items():
        noise = np.random.default_rng([zlib.crc32(name.encode()), seed]).standard_normal(out[name].shape)
        drawn = base * np.exp(spread * noise) if base else spread * noise
        out[name] = jnp.asarray(drawn.astype(out[name].dtype))
    for name, factor in factors.items():
        out[name] = (out[name] * factor).astype(out[name].dtype)
    return out
```

```python
import concourse.bass as bass
from concourse import mybir
from contextlib import ExitStack

F32 = mybir.dt.float32
F16 = mybir.dt.float16
BF16 = mybir.dt.bfloat16
I32 = mybir.dt.int32
U32 = mybir.dt.uint32
ALU = mybir.AluOpType
ACT = mybir.ActivationFunctionType
AX = mybir.AxisListType

P = 128
N0 = 2048
NL = [N0 >> l for l in range(4)]
TL = [n // P for n in NL]
QL = [max(1, n // 512) for n in NL]
CW = [min(512, n) for n in NL]
S = 2048.0
SY = 16.0
LN_EPS = 1e-5
BN_EPS = 1e-5
CLAMP = 9.0109139
PAY = 132
GL = [0, 1, 2, 3, 2, 1, 0]


class Banks:

    def __init__(self, full, free):
        self.full, self.free = full, free
        self.count = [0] * 8
        self.at = {}
        self.turn = {"aux": 0}

    def plan(self, stage, n, banks=None):
        for i in range(n):
            b = banks[i % len(banks)] if banks else 4 + self.turn["aux"] % 4
            if not banks:
                self.turn["aux"] += 1
            self.at[(stage, i)] = (b, self.count[b])
            self.count[b] += 1

    def bank(self, stage, i=0):
        return self.at[(stage, i)][0]

    def wait_free(self, pe, stage, i=0):
        b, nth = self.at[(stage, i)]
        if nth:
            pe.wait_ge(self.free[b], nth)

    def filled(self, ins, stage, i=0):
        ins.then_inc(self.full[self.at[(stage, i)][0]], 1)

    def wait_full(self, eng, stage, i=0):
        b, nth = self.at[(stage, i)]
        eng.wait_ge(self.full[b], nth + 1)

    def read(self, ins, stage, i=0):
        ins.then_inc(self.free[self.at[(stage, i)][0]], 1)


    def wait_read(self, eng, stage, i=0):
        b, nth = self.at[(stage, i)]
        eng.wait_ge(self.free[b], nth + 1)


class Steps:

    def __init__(self, eng, sem):
        self.eng, self.sem, self.n = eng, sem, 0

    def did(self, ins):
        ins.then_inc(self.sem, 1)
        self.n += 1

    def settle(self):
        self.eng.wait_ge(self.sem, self.n)


def graph_stack_kernel(nc, x, adj, sage_w, sage_b, conv_w, conv_b, pool_w, bn_g, bn_b, cat_w, out, debug=None):
    ctx = ExitStack()
    with ctx:
        def sb(name, shape, dt=F32):
            return ctx.enter_context(nc.sbuf_tensor(name, shape, dt))

        sems = {}

        def sem(name):
            if name not in sems:
                sems[name] = ctx.enter_context(nc.semaphore(name))
            return sems[name]

        atp_dram = [nc.dram_tensor(f"adjT_part{j}", [N0, N0], F16).ap() for j in range(2)]
        a_dram = {l: nc.dram_tensor(f"a{l}_rows", [NL[l], NL[l]], F32).ap() for l in (1, 2)}
        at_dram = {l: nc.dram_tensor(f"a{l}T_rows", [NL[l], NL[l]], F32).ap() for l in (1, 2)}
        sorted_dram = [nc.dram_tensor(f"sorted{l}", [NL[l], PAY], F32).ap() for l in range(3)]
        up_dram = [nc.dram_tensor(f"up{l}", [NL[l], P], F32).ap() for l in range(3)]

        ps = ctx.enter_context(nc.psum_tensor("ps", [P, 8, 512], F32))

        big = sb("big", [P, 32768])
        mid = sb("mid", [P, 14336])

        def view(base, kb, shape, dt=F32):
            size = 1
            for n in shape:
                size *= n
            words = size * (4 if dt in (F32, I32, U32) else 2) // 4
            a = base[:, int(kb * 256):int(kb * 256) + words]
            if dt != F32:
                a = a.bitcast(dt)
            if len(shape) == 2:
                a = a.rearrange("p (a b) -> p a b", a=shape[0])
            return a

        at_hi = view(big, 0, [16, N0], F16)
        at_lo = view(big, 64, [16, N0], F16)
        atp = [at_hi, at_lo]
        h_nat = view(mid, 0, [16, P])
        zT0 = view(mid, 8, [N0])
        hT = view(mid, 16, [N0])
        xh = view(mid, 24, [16, P], F16)
        xl = view(mid, 28, [16, P], F16)
        aT = {1: view(mid, 0, [8, NL[1]]), 2: view(mid, 40, [4, NL[2]]), 3: view(mid, 48, [2, NL[3]])}
        junk = view(mid, 32, [N0], BF16)
        cmp0 = [view(mid, 32, [N0], BF16), view(mid, 36, [N0], BF16)]
        iota16 = view(mid, 32, [N0], F16)
        dblk = view(mid, 36, [2, P])
        vec_rows = view(mid, 37, [P])[0:24, :]
        zeros = view(mid, 37.5, [P])
        sageb = view(mid, 38, [P])[0:1, :]
        colacc = view(mid, 40, [N0])
        xs0 = view(mid, 40, [8, PAY])
        feat1 = view(mid, 44.25, [NL[1]])
        ties = view(mid, 48, [P])
        pool_b = view(mid, 48.5, [P])
        below = view(mid, 49, [P])
        sagew = view(mid, 54, [256])
        sagewT = view(mid, 55, [256])
        diag = view(mid, 54, [4, P])
        catw = view(mid, 54, [2, P])
        srow0 = view(mid, 16, [N0])
        pay0 = view(mid, 0, [16, PAY])
        res0 = sb("res0", [P, N0])
        x_nat = sb("x_nat", [P, 16, P])
        ring = [view(mid, 8, [N0]), view(mid, 16, [N0]), view(mid, 24, [N0]), res0[:, :]]
        res = {0: res0[:, :], 1: view(mid, 36, [NL[1]]), 2: view(mid, 50, [NL[2]])}
        dn_row = {0: view(mid, 40, [N0]), 1: view(mid, 32, [NL[1]]), 2: view(mid, 52, [NL[2]]),
                  3: view(big, 127, [NL[3]])}

        sel_l = [view(big, 32 * j, [16, 1024], F16) for j in range(2)]
        sel_b = [[view(big, 64 + 8 * s + 4 * j, [16, P], F16) for j in range(2)] for s in range(3)]
        g_ring = [view(big, 88 + 8 * s, [N0]) for s in range(3)]
        b_ring = [[view(big, 112 + 8 * s + 4 * j, [N0], F16) for j in range(2)] for s in range(2)]
        gst = [view(big, 96 + 4 * s, [1024]) for s in range(2)]
        bst = [view(big, 104 + 4 * s, [1024]) for s in range(2)]
        nst = [view(big, 88 + 4 * s, [1024]) for s in range(2)]
        zTs = view(big, 112, [1024])
        ys = view(big, 116, [8, P])
        xin = view(big, 120, [1024])
        upn = view(big, 124, [8, P])
        srow_s = view(big, 64, [1024])
        cmp_s = [view(big, 68 + 2 * s, [1024], BF16) for s in range(2)]
        pay_s = view(big, 72, [8, PAY])
        xs_s = view(big, 80, [4, PAY])
        feat2 = view(big, 124, [NL[2]])
        feat3 = view(big, 126, [NL[3]])

        def lsel(l):
            return view(big, 64, [TL[l], NL[l + 1]]), view(big, 80, [TL[l], NL[l + 1]])

        ident = sb("ident", [P, P])
        ident16 = sb("ident16", [P, P], F16)
        plus_s = sb("plus_s", [P, P], F16)
        minus_s = sb("minus_s", [P, P], F16)
        ones = sb("ones", [P, P])
        ones_bf = sb("ones_bf", [P, 1], BF16)
        eps = sb("eps", [P, 2])
        index_col = sb("index_col", [P, 16])
        cw = sb("cw", [P, 7, P])
        cols = sb("cols", [P, 24])
        rnorm = sb("rnorm", [P, 6])
        stats = sb("stats", [P, 16, 6])
        mv = sb("mv", [P, 16, 2])
        lnp = sb("lnp", [P, 3, 16])
        rows = sb("rows", [P, 16])
        csum = sb("csum", [P, 3, 16])
        dn = [sb(f"dn{l}", [P, TL[l]]) for l in range(4)]
        dny = sb("dny", [P, 16])
        degs = sb("degs", [P, 3, 16])
        rsum = {l: sb(f"rsum{l}", [P, TL[l], 2]) for l in (1, 2, 3)}
        bnst = sb("bnst", [P, 4, 6])
        bnp = sb("bnp", [P, 8])
        scol = sb("scol", [P, 16])
        vals = sb("vals", [P, 16])
        rank = [sb(f"rank{l}", [P, TL[l]], I32) for l in range(3)]
        perm = [sb(f"perm{l}", [P, TL[l] // 2], I32) for l in range(3)]
        permf = sb("permf", [P, 8])

        full = [sem(f"bank{b}_full") for b in range(8)]
        free = [sem(f"bank{b}_free") for b in range(8)]
        bk = Banks(full, free)

        accs = [0, 1, 2, 3]
        bk.plan("setup", 1)
        bk.plan("pnorm", 1)
        bk.plan("msg", 4, accs)
        bk.plan("adjT", 64)
        bk.plan("csum", 1)
        bk.plan("msg_nat", 4)
        bk.plan("hT1", 4)
        bk.plan("prod1", 4, accs)
        bk.plan("out1", 4)
        bk.plan("dnrow0", 4)
        bk.plan("hT2", 4)

        def plan_gcn(g):
            q = QL[GL[g]]
            bk.plan(f"y{g}", q)
            bk.plan(f"conv{g}", q, accs)

        def plan_pool(l):
            bk.plan(f"score{l}", QL[l], accs)
            bk.plan(f"scol{l}", 1)
            bk.plan(f"pay{l}", QL[l])
            bk.plan(f"rank{l}", 1)
            bk.plan(f"xs{l}", QL[l + 1])

        plan_gcn(0)
        plan_pool(0)
        for rt in range(4):
            bk.plan(f"selL0_{rt}", 4)
        bk.plan("selB0_0", 4)
        for c in range(8):
            if c == 0:
                bk.plan("sel0_0_0", 1, [0])
                for rt in range(4, 8):
                    bk.plan(f"selL0_{rt}", 4)
                bk.plan("selB0_1", 4)
                bk.plan("sel0_0_1", 1, [1])
            else:
                if c < 7:
                    bk.plan(f"selB0_{c + 1}", 4)
                for half in range(2):
                    bk.plan(f"sel0_{c}_{half}", 1, [2 * (c % 2) + half])
        for l in (1, 2, 3):
            for rt in range(TL[l]):
                bk.plan(f"nat{l}_{rt}", QL[l])
            bk.plan(f"dnrow{l}", QL[l])
            plan_gcn(l)
            if l < 3:
                plan_pool(l)
                for rt in range(TL[l + 1]):
                    bk.plan(f"selL{l}_{rt}", QL[l])
                    bk.plan(f"selB{l}_{rt}", QL[l])
                for c in range(TL[l + 1]):
                    bk.plan(f"sel{l}_{c}", 1, [c % 4])
        for g, l in ((3, 2), (4, 1), (5, 0)):
            bk.plan(f"upnat{l}", QL[l + 1])
            bk.plan(f"upin{l}", QL[l])
            if l == 0:
                bk.plan("dnrow0b", 4)
            plan_gcn(g + 1)
        bk.plan("unet_nat", 4)
        bk.plan("hT3", 4)
        bk.plan("prod3", 4, accs)
        bk.plan("out3", 4)

        levels, down, up, convs = range(4), (1, 2), (2, 1, 0), range(7)
        signals = {
            "ln_mv": [(s, 16) for s in range(4)], "ln_std": [(s, 4) for s in range(4)],
            "ln_r": [(s, 4) for s in range(4)], "ln_h": [(s, 16) for s in range(4)],
            "x_hi": [(s, 4) for s in (1, 3)], "x_lo": [(s, 4) for s in (1, 3)],
            "y_hi": [(g, 16) for g in (0, 6)], "z": [(g, QL[GL[g]]) for g in convs],
            "bn_mv": [(g, 1) for g in convs], "bn_std": [(g, 1) for g in convs],
            "bn_par": [(g, 1) for g in convs], "bn": [(g, QL[GL[g]]) for g in convs],
            "vals": [(l, 1) for l in levels], "pay_index": [(l, 1) for l in levels],
            "srow": [(l, 1) for l in levels], "pool_b": [(l, 1) for l in levels],
            "cmp": [(l, 3 * TL[l] - 2) for l in levels], "cmp_used": [(l, TL[l] - 1) for l in levels],
            "perm": [(l, 1) for l in levels], "deg": [(l, 2) for l in levels],
            "deg_root": [(l, 1) for l in levels], "dn": [(l, 1) for l in levels],
            "dn_blocks": [("dnrow0", 16), ("dnrow1", 8), ("dnrow2", 4), ("dnrow3", 2), ("dnrow0b", 16)],
            "unit": [(l, TL[l]) for l in (1, 2, 3)], "sorted": [(l, 16 * TL[l]) for l in levels],
            "xs_in": [(l, 16) for l in levels], "aT_out": [(l, 16 * TL[l]) for l in down],
            "up_out": [(l, 16) for l in up], "up_in": [(l, 16 * TL[l]) for l in up],
        }
        for r in range(2):
            signals[f"a_out_{r}"] = [(l, 8 * TL[l]) for l in down]
            signals[f"gs_in_{r}"] = signals[f"bs_in_{r}"] = [(l, 8 * TL[l + 1]) for l in down]

        def at(name, stage, n):
            before = 0
            for s, total in signals[name]:
                if s == stage:
                    return sem(name), before + n
                before += total
            raise KeyError((name, stage))

        def aux(stage, i=0):
            return ps[:, bk.bank(stage, i), :]

        def xin_of(g):
            return {0: hT, 1: feat1, 2: feat2, 3: feat3, 4: xin, 5: xin, 6: hT}[g]

        def z_of(g):
            return zT0 if GL[g] == 0 else zTs

        def bn_out(g):
            return {0: res[0], 1: res[1], 2: res[2], 3: zTs, 4: zTs, 5: zTs, 6: zT0}[g]

        def scratch(l):
            if l == 0:
                return srow0, cmp0, pay0, xs0
            return srow_s, cmp_s, pay_s, xs_s

        def blk(t):
            return slice((t % 4) * P, (t % 4 + 1) * P)

        def chunk_tiles(l, q):
            return range(4 * q, min(4 * q + 4, TL[l]))

        def ring_row_in(eng, it):
            eng.wait_ge(sem(f"row_in{it % 4}"), 16 * (it // 4 + 1))

        def sel_read(eng, l, c):
            if l == 1:
                bk.wait_read(eng, f"sel0_{c}_0")
                bk.wait_read(eng, f"sel0_{c}_1")
            else:
                bk.wait_read(eng, f"sel{l - 1}_{c}")

        def cmps(l, t):
            return 3 * (t + 1) - 1 - (1 if t == TL[l] - 1 else 0)

        block = ctx.enter_context(nc.Block())

        @block.sync
        def _(sp):
            sp.dma_start(x_nat[:, :, :], x.rearrange("(t p) d -> p t d", p=P)).then_inc(sem("x_in"), 16)
            sp.dma_start(vec_rows[0:7, :], conv_b).then_inc(sem("vec_in"), 16)
            sp.dma_start(vec_rows[7:14, :], bn_g).then_inc(sem("vec_in"), 16)
            sp.dma_start(vec_rows[14:21, :], bn_b).then_inc(sem("vec_in"), 16)
            sp.dma_start(vec_rows[21:24, :], pool_w).then_inc(sem("vec_in"), 16)
            sp.dma_start(sagew, sage_w).then_inc(sem("vec_in"), 16)
            for it in range(16):
                if it >= 4:
                    sp.wait_ge(sem("row_used_pe"), it - 3)
                    if it % 2:
                        sp.wait_ge(sem("rows_dve"), (it - 4) // 2 + 1)
                    else:
                        sp.wait_ge(sem("rows_act"), (it - 4) // 2 + 1)
                    sp.wait_ge(sem("colacc"), it - 3)
                sp.dma_start(ring[it % 4], adj[it * P:(it + 1) * P, :]).then_inc(sem(f"row_in{it % 4}"), 16)
                if it == 3:
                    sp.dma_start(cw[:, :, :], conv_w.rearrange("g c o -> c g o")).then_inc(sem("w_in"), 16)
                    sp.dma_start(sageb, sage_b.rearrange("(a o) -> a o", a=1)).then_inc(sem("w_in"), 16)
            sp.wait_ge(sem("zeros"), 1)
            for l in range(3):
                for t in range(TL[l + 1], TL[l]):
                    sp.dma_start(up_dram[l][t * P:(t + 1) * P, :], zeros).then_inc(sem("zeros_out"), 16)
            sp.wait_ge(sem("at_hi"), 64)
            bk.wait_read(sp, "adjT", 60)
            bk.wait_read(sp, "adjT", 61)
            bk.wait_read(sp, "adjT", 62)
            bk.wait_read(sp, "adjT", 63)
            for j in range(2):
                for jt in range(0, 16, 4):
                    sp.dma_start(atp_dram[j][jt * P:(jt + 4) * P, :].rearrange("(t p) k -> p t k", p=P),
                                 atp[j][:, jt:jt + 4, :]).then_inc(sem("at_out"), 16)

            def sorted_in(l):
                sp.wait_ge(*at("sorted", l, 16 * TL[l]))
                sp.dma_start(scratch(l)[3][:, 0:TL[l + 1], :],
                             sorted_dram[l][0:NL[l + 1], :].rearrange("(t p) d -> p t d", p=P))\
                    .then_inc(sem("xs_in"), 16)

            def rows_out(l):
                for c in range(TL[l]):
                    sp.wait_ge(*at("unit", l, c + 1))
                    sel_read(sp, l, c)
                    sp.dma_start(at_dram[l][c * P:(c + 1) * P, :], aT[l][:, c, :]).then_inc(sem("aT_out"), 16)
                for rt in range(TL[l]):
                    for q in range(QL[l]):
                        bk.wait_read(sp, f"nat{l}_{rt}", q)
                    sp.dma_start(a_dram[l][rt * P:(rt + 1) * P, :], nst[rt % 2][:, 0:NL[l]])\
                        .then_inc(sem(f"a_out_{rt % 2}"), 16)

            def up_out(l):
                for q in range(QL[l + 1]):
                    bk.wait_read(sp, f"upnat{l}", q)
                sp.dma_start(up_dram[l][0:NL[l + 1], :].rearrange("(t p) d -> p t d", p=P),
                             upn[:, 0:TL[l + 1], :]).then_inc(sem("up_out"), 16)

            sorted_in(0)
            rows_out(1)
            for half in range(2):
                bk.wait_full(sp, f"sel0_7_{half}")
            for jt in range(0, 16, 4):
                sp.dma_start(at_hi[:, jt:jt + 4, :],
                             atp_dram[0][jt * P:(jt + 4) * P, :].rearrange("(t p) k -> p t k", p=P))\
                    .then_inc(sem("at_hi_back"), 16)
            sorted_in(1)
            rows_out(2)
            sorted_in(2)
            up_out(2)
            up_out(1)
            up_out(0)
            sp.wait_ge(*at("up_out", 0, 16))
            for jt in range(0, 16, 4):
                sp.dma_start(at_lo[:, jt:jt + 4, :],
                             atp_dram[1][jt * P:(jt + 4) * P, :].rearrange("(t p) k -> p t k", p=P))\
                    .then_inc(sem("at_lo_back"), 16)
            for q in range(4):
                bk.wait_full(sp, "dnrow0b", q)
            sp.dma_start(catw, cat_w.rearrange("(a c) o -> c a o", a=2)).then_inc(sem("catw_in"), 16)
            for q in range(4):
                bk.wait_read(sp, "out3", q)
                sp.dma_start(out[q * 512:(q + 1) * 512, :].rearrange("(t p) d -> p t d", p=P),
                             x_nat[:, 4 * q:4 * q + 4, :]).then_inc(sem("out"), 16)
            sp.wait_ge(sem("out"), 64)

        @block.gpsimd
        def _(pool):
            for tile in (ident[:, :], ident16[:, :], plus_s[:, :], minus_s[:, :], below):
                nc.gpsimd.memset(tile, 0.0).then_inc(sem("cleared"), 1)
            nc.gpsimd.memset(ones[:, :], 1.0).then_inc(sem("ones"), 1)
            nc.gpsimd.memset(ones_bf[:, :], 1.0).then_inc(sem("ones"), 1)
            pool.wait_ge(sem("cleared"), 5)
            for tile, fill, op in ((ident[:, :], 1.0, ALU.not_equal), (ident16[:, :], 1.0, ALU.not_equal),
                                   (plus_s[:, :], S, ALU.not_equal), (minus_s[:, :], -S, ALU.not_equal),
                                   (below, 1.0, ALU.is_ge)):
                nc.gpsimd.affine_select(out=tile, in_=tile, compare_op=op, fill=fill,
                                        base=0, pattern=[[-1, P]], channel_multiplier=1)\
                    .then_inc(sem("consts"), 1)
            nc.gpsimd.iota(index_col[:, :], pattern=[[P, 16]], base=0, channel_multiplier=1,
                           allow_small_or_imprecise_dtypes=True).then_inc(sem("index_col"), 1)
            nc.gpsimd.memset(zeros, 0.0).then_inc(sem("zeros"), 1)
            pool.wait_ge(sem("consts"), 5)
            for it in range(16):
                ring_row_in(pool, it)
                if it >= 2:
                    pool.wait_ge(sem("row_used_pe"), it - 1)
                a = ring[it % 4]
                nc.gpsimd.tensor_tensor(dblk[:, it % 2, :], a[:, it * P:(it + 1) * P], ident[:, :], ALU.add)\
                    .then_inc(sem("dblk"), 1)
                if it:
                    pool.wait_ge(sem("colacc"), it)
                    nc.gpsimd.tensor_tensor(colacc, colacc, a, ALU.add).then_inc(sem("colacc"), 1)
                else:
                    nc.gpsimd.tensor_copy(colacc, a).then_inc(sem("colacc"), 1)

            def gather(dst, src, index, done):
                nc.gpsimd.indirect_dma_start(
                    out=dst, out_offset=None, in_=src,
                    in_offset=bass.IndirectOffsetOnAxis(index, 0)).then_inc(done, 16)

            def scatter(l):
                pool.wait_ge(*at("pay_index", l, 1))
                for q in range(QL[l]):
                    bk.wait_read(pool, f"pay{l}", q)
                bk.wait_read(pool, f"rank{l}")
                for t in range(TL[l]):
                    nc.gpsimd.indirect_dma_start(
                        out=sorted_dram[l],
                        out_offset=bass.IndirectOffsetOnAxis(rank[l][:, t:t + 1].bitcast(U32), 0),
                        in_=scratch(l)[2][:, t, :], in_offset=None).then_inc(sem("sorted"), 16)

            def unit_diag(l, c):
                sel_read(pool, l, c)
                b = aT[l][:, c, c * P:(c + 1) * P]
                nc.gpsimd.affine_select(out=b, in_=b, compare_op=ALU.not_equal, fill=1.0,
                                        base=0, pattern=[[-1, P]], channel_multiplier=1)\
                    .then_inc(sem("unit"), 1)

            scatter(0)
            nc.gpsimd.iota(iota16, pattern=[[1, N0]], base=0, channel_multiplier=0,
                           allow_small_or_imprecise_dtypes=True).then_inc(sem("iota16"), 1)
            pool.wait_ge(*at("perm", 0, 1))
            pool.wait_ge(sem("at_out"), 128)

            def p0(c):
                return perm[0][:, c:c + 1].bitcast(U32)

            def gather_l0(rt):
                if rt >= 3:
                    bk.wait_full(pool, f"selL0_{rt - 3}", 3)
                gather(g_ring[rt % 3], adj, p0(rt), sem(f"g_in{rt % 3}"))

            def gather_b0(c):
                if c >= 2:
                    bk.wait_full(pool, f"selB0_{c - 2}", 3)
                for j in range(2):
                    gather(b_ring[c % 2][j], atp_dram[j], p0(c), sem(f"b_in{c % 2}"))

            for rt in range(3):
                gather_l0(rt)
            gather_b0(0)
            gather_l0(3)
            gather_b0(1)
            for rt in range(4, 8):
                gather_l0(rt)
            for c in range(8):
                if c + 2 < 8:
                    gather_b0(c + 2)
                unit_diag(1, c)
            for l in (1, 2):
                scatter(l)
                pool.wait_ge(*at("perm", l, 1))
                pool.wait_ge(*at("aT_out", l, 16 * TL[l]))
                for r in range(2):
                    pool.wait_ge(*at(f"a_out_{r}", l, 16 * TL[l] // 2))
                for rt in range(TL[l + 1]):
                    if rt >= 2:
                        for q in range(QL[l]):
                            bk.wait_full(pool, f"selL{l}_{rt - 2}", q)
                            bk.wait_full(pool, f"selB{l}_{rt - 2}", q)
                    pl = perm[l][:, rt:rt + 1].bitcast(U32)
                    gather(gst[rt % 2][:, 0:NL[l]], a_dram[l], pl, sem(f"gs_in_{rt % 2}"))
                    gather(bst[rt % 2][:, 0:NL[l]], at_dram[l], pl, sem(f"bs_in_{rt % 2}"))
                for c in range(TL[l + 1]):
                    unit_diag(l + 1, c)
            pool.wait_ge(sem("zeros_out"), 16 * (8 + 4 + 2))
            for l in (2, 1, 0):
                pool.wait_ge(*at("up_out", l, 16))
                for t in range(TL[l]):
                    gather(h_nat[:, t, :] if l == 0 else upn[:, t, :], up_dram[l],
                           rank[l][:, t:t + 1].bitcast(U32), sem("up_in"))

        @block.scalar
        def _(act):
            def copy_out(stage, i, dst, src, **kw):
                bk.wait_full(act, stage, i)
                bk.read(nc.scalar.activation(dst, src, ACT.Copy, **kw), stage, i)

            def layernorm(s, split):
                def std(c):
                    cs = slice(4 * c, 4 * c + 4)
                    act.wait_ge(*at("ln_mv", s, 4 * c + 4))
                    nc.scalar.activation(lnp[:, 0, cs], mv[:, cs, 1], ACT.Sqrt, bias=eps[:, 0:1])\
                        .then_inc(sem("ln_std"), 1)

                def rest(c):
                    act.wait_ge(*at("ln_r", s, c + 1))
                    for t in range(4 * c, 4 * c + 4):
                        nc.scalar.activation(h_nat[:, t, :], x_nat[:, t, :], ACT.Relu,
                                             bias=lnp[:, 2, t:t + 1], scale=lnp[:, 1, t:t + 1])\
                            .then_inc(sem("ln_h"), 1)
                    if split:
                        act.wait_ge(*at("ln_h", s, 4 * c + 4))
                        nc.scalar.activation(xh[:, 4 * c:4 * c + 4, :], h_nat[:, 4 * c:4 * c + 4, :],
                                             ACT.Copy, scale=S).then_inc(sem("x_hi"), 1)

                std(0)
                for c in range(1, 4):
                    std(c)
                    rest(c - 1)
                rest(3)

            bk.wait_full(act, "setup")
            nc.scalar.activation(sagewT, aux("setup")[:, 0:256], ACT.Copy).then_inc(sem("sagewT"), 1)
            bk.read(nc.scalar.activation(cols[:, :], aux("setup")[:, 256:280], ACT.Copy), "setup")
            bk.wait_full(act, "pnorm")
            bk.read(nc.scalar.activation(rnorm[:, 3:6], aux("pnorm")[:, 0:3], ACT.Sqrt), "pnorm")
            act.wait_ge(sem("eps"), 2)
            layernorm(0, False)

            for it in range(16):
                for q in range(4):
                    bk.wait_full(act, "adjT", 4 * it + q)
                    nc.scalar.activation(at_hi[:, 4 * q:4 * q + 4, it * P:(it + 1) * P],
                                         aux("adjT", 4 * it + q).rearrange("p (a b) -> p a b", a=4),
                                         ACT.Copy, scale=S).then_inc(sem("at_hi"), 1)
                if it % 2 == 0:
                    if it:
                        act.wait_ge(sem("rows_act"), it // 2)
                    nc.scalar.activation(junk, ring[it % 4], ACT.Copy, accum_out=rows[:, it:it + 1])\
                        .then_inc(sem("rows_act"), 1)
            bk.wait_full(act, "msg", 3)
            act.wait_ge(sem("colacc"), 16)
            act.wait_ge(sem("rows_dve"), 8)
            act.wait_ge(sem("rows_act"), 8)
            for q in range(4):
                copy_out("msg", q, zT0[:, q * 512:(q + 1) * 512], ps[:, q, :])

            def hT_out(stage):
                for q in range(4):
                    copy_out(stage, q, hT[:, q * 512:(q + 1) * 512], aux(stage, q))

            def product_out(stage):
                for q in range(4):
                    copy_out(stage, q, zT0[:, q * 512:(q + 1) * 512], ps[:, q, :], scale=1.0 / (S * S))

            def degree_root(l):
                act.wait_ge(*at("deg", l, 2))
                nc.scalar.activation(degs[:, 1, 0:TL[l]], degs[:, 0, 0:TL[l]], ACT.Sqrt)\
                    .then_inc(sem("deg_root"), 1)

            def dn_row_out(l, stage):
                for q in range(QL[l]):
                    copy_out(stage, q, dn_row[l][:, q * CW[l]:(q + 1) * CW[l]], aux(stage, q)[:, 0:CW[l]],
                             scale=1.0 / (S * SY) if l == 0 else 1.0)

            def conv(g):
                l, w = GL[g], CW[GL[g]]
                act.wait_ge(*at("dn", l, 1))
                if l == 0:
                    act.wait_ge(sem("dny"), 1)
                for q in range(QL[l]):
                    bk.wait_full(act, f"y{g}", q)
                    ts = chunk_tiles(l, q)
                    for t in ts:
                        src = aux(f"y{g}", q)[:, blk(t)]
                        if l == 0:
                            nc.scalar.activation(xh[:, t, :], src, ACT.Copy, scale=dny[:, t:t + 1])\
                                .then_inc(sem("y_hi"), 1)
                        else:
                            ins = nc.scalar.activation(ys[:, t, :], src, ACT.Copy, scale=dn[l][:, t:t + 1])
                            if t == ts[-1]:
                                bk.read(ins, f"y{g}", q)
                for q in range(QL[l]):
                    bk.wait_read(act, f"conv{g}", q)
                    z = z_of(g)[:, q * w:(q + 1) * w]
                    nc.scalar.activation(z, z, ACT.Identity if g == 6 else ACT.Relu, bias=cols[:, g:g + 1])\
                        .then_inc(sem("z"), 1)
                act.wait_ge(*at("bn_mv", g, 1))
                nc.scalar.activation(bnp[:, 2:3], bnp[:, 1:2], ACT.Sqrt, bias=eps[:, 1:2])\
                    .then_inc(sem("bn_std"), 1)
                act.wait_ge(*at("bn_par", g, 1))
                for q in range(QL[l]):
                    sl = slice(q * w, (q + 1) * w)
                    nc.scalar.activation(bn_out(g)[:, sl], z_of(g)[:, sl], ACT.Identity,
                                         bias=bnp[:, 5:6], scale=bnp[:, 4:5]).then_inc(sem("bn"), 1)

            def pooling(l):
                bk.wait_read(act, f"scol{l}")
                nc.scalar.activation(vals[:, 0:TL[l]], scol[:, 0:TL[l]], ACT.Tanh).then_inc(sem("vals"), 1)
                act.wait_ge(*at("vals", l, 1))
                pay = scratch(l)[2]
                for q in range(QL[l]):
                    bk.wait_full(act, f"pay{l}", q)
                    ts = chunk_tiles(l, q)
                    for t in ts:
                        ins = nc.scalar.activation(pay[:, t, 0:P], aux(f"pay{l}", q)[:, blk(t)],
                                                   ACT.Copy, scale=vals[:, t:t + 1])
                        if t == ts[-1]:
                            bk.read(ins, f"pay{l}", q)
                act.wait_ge(sem("index_col"), 1)
                nc.scalar.activation(pay[:, 0:TL[l], P:PAY],
                                     index_col[:, 0:TL[l]].unsqueeze(2).to_broadcast([P, TL[l], PAY - P]), ACT.Copy)\
                    .then_inc(sem("pay_index"), 1)

            def kept_features(l):
                dst = {0: feat1, 1: feat2, 2: feat3}[l]
                for q in range(QL[l + 1]):
                    w = CW[l + 1]
                    copy_out(f"xs{l}", q, dst[:, q * w:(q + 1) * w], aux(f"xs{l}", q)[:, 0:w])

            def natural_rows(l):
                for rt in range(TL[l]):
                    if rt >= 2 and l < 3:
                        act.wait_ge(*at(f"a_out_{rt % 2}", l, 16 * (rt // 2)))
                    w = CW[l]
                    for q in range(QL[l]):
                        bk.wait_full(act, f"nat{l}_{rt}", q)
                        bk.read(nc.scalar.activation(nst[rt % 2][:, q * w:(q + 1) * w],
                                                     aux(f"nat{l}_{rt}", q)[:, 0:w], ACT.Copy,
                                                     accum_out=rsum[l][:, rt, q:q + 1]), f"nat{l}_{rt}", q)

            layernorm(1, True)
            hT_out("hT1")
            product_out("prod1")
            degree_root(0)
            dn_row_out(0, "dnrow0")
            layernorm(2, False)
            hT_out("hT2")
            conv(0)
            pooling(0)
            kept_features(0)

            def sel_l0(rt):
                for q in range(4):
                    bk.wait_full(act, f"selL0_{rt}", q)
                    nc.scalar.activation(sel_l[0][:, 4 * q:4 * q + 4, rt * P:(rt + 1) * P],
                                         aux(f"selL0_{rt}", q).rearrange("p (a b) -> p a b", a=4), ACT.Copy, scale=S)\
                        .then_inc(sem("sel_hi"), 1)

            def sel_b0(c):
                if c >= 3:
                    for half in range(2):
                        bk.wait_full(act, f"sel0_{c - 3}_{half}")
                for q in range(2):
                    copy_out(f"selB0_{c}", q, sel_b[c % 3][0][:, 8 * q:8 * q + 8, :].rearrange("p a b -> p (a b)"),
                             aux(f"selB0_{c}", q).bitcast(F16))

            def sel0_out(c):
                for half in range(2):
                    copy_out(f"sel0_{c}_{half}", 0, aT[1][:, c, half * 512:(half + 1) * 512],
                             ps[:, bk.bank(f"sel0_{c}_{half}"), :], scale=1.0 / (S * S))

            for rt in range(4):
                sel_l0(rt)
            sel_b0(0)
            for rt in range(4, 8):
                sel_l0(rt)
            sel_b0(1)
            sel0_out(0)
            for c in range(1, 8):
                if c < 7:
                    sel_b0(c + 1)
                sel0_out(c)

            def up_natural(l):
                for q in range(QL[l + 1]):
                    n = len(chunk_tiles(l + 1, q))
                    copy_out(f"upnat{l}", q, upn[:, 4 * q:4 * q + n, :].rearrange("p a b -> p (a b)"),
                             aux(f"upnat{l}", q)[:, 0:n * P])

            for l in (1, 2, 3):
                natural_rows(l)
                degree_root(l)
                dn_row_out(l, f"dnrow{l}")
                conv(l)
                if l < 3:
                    pooling(l)
                    kept_features(l)
                    for rt in range(TL[l + 1]):
                        for q in range(QL[l]):
                            n = len(chunk_tiles(l, q))
                            copy_out(f"selL{l}_{rt}", q, lsel(l)[0][:, 4 * q:4 * q + n, rt * P:(rt + 1) * P],
                                     aux(f"selL{l}_{rt}", q)[:, 0:n * P].rearrange("p (a b) -> p a b", a=n))
                    for c in range(TL[l + 1]):
                        copy_out(f"sel{l}_{c}", 0, aT[l + 1][:, c, :], ps[:, c % 4, 0:NL[l + 1]])
            for g, l in ((3, 2), (4, 1), (5, 0)):
                up_natural(l)
                if l == 0:
                    dn_row_out(0, "dnrow0b")
                conv(g + 1)
            layernorm(3, True)
            hT_out("hT3")
            product_out("prod3")

        @block.vector
        def _(dve):
            own = Steps(dve, sem("dve_own"))
            V = nc.vector

            V.memset(eps[:, 0:1], LN_EPS).then_inc(sem("eps"), 1)
            V.memset(eps[:, 1:2], BN_EPS).then_inc(sem("eps"), 1)

            def layernorm(s, ready, split):
                def moments(c):
                    ready(c)
                    for t in range(4 * c, 4 * c + 4):
                        own.did(V.bn_stats(stats[:, t, :], x_nat[:, t, :]))
                    own.settle()
                    for t in range(4 * c, 4 * c + 4):
                        V.bn_aggr(mv[:, t, :], stats[:, t, :]).then_inc(sem("ln_mv"), 1)

                def rest(c):
                    cs = slice(4 * c, 4 * c + 4)
                    dve.wait_ge(*at("ln_std", s, c + 1))
                    own.did(V.reciprocal(lnp[:, 1, cs], lnp[:, 0, cs]))
                    own.settle()
                    V.scalar_tensor_tensor(lnp[:, 2, cs], mv[:, cs, 0], -1.0, lnp[:, 1, cs], ALU.mult, ALU.mult)\
                        .then_inc(sem("ln_r"), 1)

                def low(c):
                    cs = slice(4 * c, 4 * c + 4)
                    dve.wait_ge(*at("x_hi", s, c + 1))
                    V.scalar_tensor_tensor(xl[:, cs, :].rearrange("p a b -> p (a b)"),
                                           h_nat[:, cs, :].rearrange("p a b -> p (a b)"), S,
                                           xh[:, cs, :].rearrange("p a b -> p (a b)"), ALU.mult, ALU.subtract)\
                        .then_inc(sem("x_lo"), 1)

                moments(0)
                for c in range(1, 4):
                    moments(c)
                    rest(c - 1)
                    if split and c >= 2:
                        low(c - 2)
                rest(3)
                if split:
                    low(2)
                    low(3)

            bk.wait_read(dve, "setup")
            V.tensor_tensor(degs[:, 0, 0:3], cols[:, 21:24], cols[:, 21:24], ALU.mult).then_inc(sem("pool_sq"), 1)
            bk.wait_read(dve, "pnorm")
            own.did(V.reciprocal(rnorm[:, 0:3], rnorm[:, 3:6]))
            layernorm(0, lambda c: dve.wait_ge(sem("x_in"), 16), False)

            for it in range(16):
                for q in range(4):
                    u = 4 * it + q
                    dve.wait_ge(sem("at_hi"), u + 1)
                    dst = [a[:, 4 * q:4 * q + 4, it * P:(it + 1) * P] for a in atp]
                    bk.read(V.scalar_tensor_tensor(dst[1], aux("adjT", u).rearrange("p (a b) -> p a b", a=4), S,
                                                   dst[0], ALU.mult, ALU.subtract), "adjT", u)
                if it % 2:
                    V.reduce_sum(rows[:, it:it + 1], ring[it % 4], axis=AX.X).then_inc(sem("rows_dve"), 1)

            bk.wait_full(dve, "csum")
            bk.read(V.tensor_copy(csum[:, 0, :], aux("csum")[:, 0:16]), "csum")
            bk.wait_read(dve, "csum")
            own.did(V.tensor_scalar(csum[:, 1, :], csum[:, 0, :], 0.0, None, ALU.is_equal))
            own.settle()
            own.did(V.tensor_tensor(csum[:, 0, :], csum[:, 0, :], csum[:, 1, :], ALU.add))
            own.did(V.tensor_scalar(csum[:, 2, :], csum[:, 1, :], -1.0, 1.0, ALU.mult, ALU.add))
            own.settle()
            own.did(V.reciprocal(csum[:, 1, :], csum[:, 0, :]))
            own.settle()
            own.did(V.tensor_tensor(csum[:, 0, :], csum[:, 1, :], csum[:, 2, :], ALU.mult))
            own.settle()
            for q in range(4):
                bk.wait_full(dve, "msg_nat", q)
                for t in range(4 * q, 4 * q + 4):
                    ins = V.scalar_tensor_tensor(x_nat[:, t, :], aux("msg_nat", q)[:, blk(t)], csum[:, 0, t:t + 1],
                                                 x_nat[:, t, :], ALU.mult, ALU.add)
                bk.read(ins, "msg_nat", q)
            layernorm(1, lambda c: bk.wait_read(dve, "msg_nat", c), True)

            def degrees(l):
                n = TL[l]
                if l == 0:
                    dve.wait_ge(sem("rows_act"), 8)
                    dve.wait_ge(sem("rows_dve"), 8)
                    own.did(V.tensor_scalar(degs[:, 0, :], rows[:, :], 2.0, None, ALU.add))
                else:
                    for rt in range(n):
                        for q in range(QL[l]):
                            bk.wait_read(dve, f"nat{l}_{rt}", q)
                    if QL[l] == 2:
                        own.did(V.scalar_tensor_tensor(degs[:, 0, 0:n], rsum[l][:, :, 0], 1.0, rsum[l][:, :, 1],
                                                       ALU.add, ALU.add))
                    else:
                        own.did(V.tensor_scalar(degs[:, 0, 0:n], rsum[l][:, :, 0], 1.0, None, ALU.add))
                own.settle()
                V.tensor_scalar(degs[:, 2, 0:n], degs[:, 0, 0:n], 0.0, None, ALU.is_gt).then_inc(sem("deg"), 1)
                dve.wait_ge(*at("deg", l, 1))
                V.tensor_scalar(degs[:, 0, 0:n], degs[:, 0, 0:n], 1e-30, None, ALU.max).then_inc(sem("deg"), 1)
                dve.wait_ge(*at("deg_root", l, 1))
                own.did(V.reciprocal(degs[:, 1, 0:n], degs[:, 1, 0:n]))
                own.settle()
                V.tensor_tensor(dn[l][:, :], degs[:, 1, 0:n], degs[:, 2, 0:n], ALU.mult).then_inc(sem("dn"), 1)
                dve.wait_ge(*at("dn", l, 1))
                if l == 0:
                    V.tensor_scalar(dny[:, :], dn[0][:, :], SY, None, ALU.mult).then_inc(sem("dny"), 1)

            def dn_blocks(l, stage):
                for q in range(QL[l]):
                    if q:
                        bk.wait_full(dve, stage, q - 1)
                    for t in chunk_tiles(l, q):
                        V.tensor_scalar(diag[:, t % 4, :], ident[:, :], dn[l][:, t:t + 1], None, ALU.mult)\
                            .then_inc(sem("dn_blocks"), 1)

            for q in range(4):
                bk.wait_full(dve, "out1", q)
                xc = x_nat[:, 4 * q:4 * q + 4, :].rearrange("p a b -> p (a b)")
                bk.read(V.scalar_tensor_tensor(xc, aux("out1", q), 0.0, xc, ALU.max, ALU.add), "out1", q)
            degrees(0)
            dn_blocks(0, "dnrow0")
            layernorm(2, lambda c: bk.wait_read(dve, "out1", c), False)

            def conv(g, stage_dn):
                l, w = GL[g], CW[GL[g]]
                if l == 0:
                    for q in range(4):
                        dve.wait_ge(*at("y_hi", g, 4 * q + 4))
                        dve.wait_ge(sem("dny"), 1)
                        for t in chunk_tiles(0, q):
                            ins = V.scalar_tensor_tensor(xl[:, t, :], aux(f"y{g}", q)[:, blk(t)], dny[:, t:t + 1],
                                                         xh[:, t, :], ALU.mult, ALU.subtract)
                        bk.read(ins, f"y{g}", q)
                for q in range(QL[l]):
                    bk.wait_read(dve, stage_dn, q)
                    bk.wait_full(dve, f"conv{g}", q)
                    sl = slice(q * w, (q + 1) * w)
                    bk.read(V.tensor_tensor(z_of(g)[:, sl], ps[:, q, 0:w], dn_row[l][:, sl], ALU.mult), f"conv{g}", q)
                for q in range(QL[l]):
                    dve.wait_ge(*at("z", g, q + 1))
                    own.did(V.bn_stats(bnst[:, q, :], z_of(g)[:, q * w:(q + 1) * w]))
                own.settle()
                V.bn_aggr(bnp[:, 0:2], bnst[:, 0:QL[l], :]).then_inc(sem("bn_mv"), 1)
                dve.wait_ge(*at("bn_std", g, 1))
                own.did(V.reciprocal(bnp[:, 3:4], bnp[:, 2:3]))
                own.settle()
                own.did(V.tensor_tensor(bnp[:, 4:5], bnp[:, 3:4], cols[:, 7 + g:8 + g], ALU.mult))
                own.settle()
                own.did(V.tensor_tensor(bnp[:, 6:7], bnp[:, 0:1], bnp[:, 4:5], ALU.mult))
                own.settle()
                V.tensor_tensor(bnp[:, 5:6], cols[:, 14 + g:15 + g], bnp[:, 6:7], ALU.subtract)\
                    .then_inc(sem("bn_par"), 1)

            def pooling(l):
                n, w = NL[l], CW[l]
                srow, cmp, _, xs = scratch(l)
                V.tensor_scalar(pool_b, ones[:, :], cols[:, 21 + l:22 + l], None, ALU.mult).then_inc(sem("pool_b"), 1)
                for q in range(QL[l]):
                    bk.wait_full(dve, f"score{l}", q)
                    bk.read(V.tensor_scalar(srow[:, q * w:(q + 1) * w], ps[:, q, 0:w], rnorm[:, l:l + 1], CLAMP,
                                            ALU.mult, ALU.min), f"score{l}", q)
                for q in range(QL[l]):
                    bk.wait_read(dve, f"score{l}", q)
                V.tensor_scalar(srow[:, 0:n], srow[:, 0:n], -CLAMP, None, ALU.max).then_inc(sem("srow"), 1)
                bk.wait_full(dve, f"scol{l}")
                bk.read(V.tensor_copy(scol[:, 0:TL[l]], aux(f"scol{l}")[:, 0:TL[l]]), f"scol{l}")
                bk.wait_read(dve, f"scol{l}")
                if l == 0:
                    dve.wait_ge(sem("zeros_out"), 16 * 14)
                for t in range(TL[l]):
                    m, a, b = cmp[t % 2], t * P, (t + 1) * P
                    if t >= 2:
                        dve.wait_ge(*at("cmp_used", l, t - 1))
                    own.did(V.scalar_tensor_tensor(ties, srow[:, a:b], scol[:, t:t + 1], below,
                                                   ALU.is_equal, ALU.mult))
                    if a:
                        V.tensor_scalar(m[:, 0:a], srow[:, 0:a], scol[:, t:t + 1], None, ALU.is_lt)\
                            .then_inc(sem("cmp"), 1)
                    if b < n:
                        V.tensor_scalar(m[:, b:n], srow[:, b:n], scol[:, t:t + 1], None, ALU.is_le)\
                            .then_inc(sem("cmp"), 1)
                    own.settle()
                    V.scalar_tensor_tensor(m[:, a:b], srow[:, a:b], scol[:, t:t + 1], ties, ALU.is_lt, ALU.add)\
                        .then_inc(sem("cmp"), 1)
                    dve.wait_ge(*at("cmp", l, cmps(l, t)))
                bk.wait_full(dve, f"rank{l}")
                bk.read(V.tensor_copy(rank[l][:, :], aux(f"rank{l}")[:, 0:TL[l]]), f"rank{l}")
                dve.wait_ge(*at("xs_in", l, 16))
                k = TL[l + 1]
                if l == 0:
                    own.did(V.tensor_copy(permf[:, 0:k], xs[:, 0:k, P]))
                V.tensor_copy(perm[l][:, :], xs[:, 0:k, P]).then_inc(sem("perm"), 1)

            conv(0, "dnrow0")
            pooling(0)

            def sel_l0(rt):
                dve.wait_ge(sem(f"g_in{rt % 3}"), 16 * (rt // 3 + 1))
                g = g_ring[rt % 3]
                V.scalar_tensor_tensor(g, iota16, permf[:, rt:rt + 1], g, ALU.is_equal, ALU.add)\
                    .then_inc(sem("g_unit"), 1)

            def sel_l0_low(rt):
                for q in range(4):
                    dve.wait_ge(sem("sel_hi"), 4 * rt + q + 1)
                    dst = [a[:, 4 * q:4 * q + 4, rt * P:(rt + 1) * P] for a in sel_l]
                    bk.read(V.scalar_tensor_tensor(dst[1], aux(f"selL0_{rt}", q).rearrange("p (a b) -> p a b", a=4),
                                                   S, dst[0], ALU.mult, ALU.subtract), f"selL0_{rt}", q)

            def sel_b0(c):
                if c >= 3:
                    for half in range(2):
                        bk.wait_full(dve, f"sel0_{c - 3}_{half}")
                for q in range(2):
                    bk.wait_full(dve, f"selB0_{c}", 2 + q)
                    bk.read(V.tensor_copy(sel_b[c % 3][1][:, 8 * q:8 * q + 8, :].rearrange("p a b -> p (a b)"),
                                          aux(f"selB0_{c}", 2 + q).bitcast(F16)), f"selB0_{c}", 2 + q)

            dve.wait_ge(sem("iota16"), 1)
            own.settle()
            sel_l0(0)
            for rt in range(1, 4):
                sel_l0(rt)
                sel_l0_low(rt - 1)
            sel_l0_low(3)
            sel_b0(0)
            sel_l0(4)
            for rt in range(5, 8):
                sel_l0(rt)
                sel_l0_low(rt - 1)
            sel_l0_low(7)
            for c in range(1, 8):
                sel_b0(c)

            for l in (1, 2, 3):
                degrees(l)
                dn_blocks(l, f"dnrow{l}")
                conv(l, f"dnrow{l}")
                if l < 3:
                    pooling(l)
                    for rt in range(TL[l + 1]):
                        for q in range(QL[l]):
                            n = len(chunk_tiles(l, q))
                            bk.wait_full(dve, f"selB{l}_{rt}", q)
                            bk.read(V.tensor_copy(lsel(l)[1][:, 4 * q:4 * q + n, rt * P:(rt + 1) * P],
                                                  aux(f"selB{l}_{rt}", q)[:, 0:n * P]
                                                  .rearrange("p (a b) -> p a b", a=n)), f"selB{l}_{rt}", q)
            for g, l in ((3, 2), (4, 1), (5, 0)):
                for q in range(QL[l]):
                    bk.wait_full(dve, f"upin{l}", q)
                    sl = slice(q * CW[l], (q + 1) * CW[l])
                    bk.read(V.tensor_tensor(xin_of(g + 1)[:, sl], aux(f"upin{l}", q)[:, 0:CW[l]], res[l][:, sl],
                                            ALU.add), f"upin{l}", q)
                if l == 0:
                    dn_blocks(0, "dnrow0b")
                conv(g + 1, "dnrow0b" if l == 0 else f"dnrow{l}")
            for q in range(4):
                bk.wait_full(dve, "unet_nat", q)
                xc = x_nat[:, 4 * q:4 * q + 4, :].rearrange("p a b -> p (a b)")
                bk.read(V.tensor_tensor(xc, aux("unet_nat", q), xc, ALU.add), "unet_nat", q)
            layernorm(3, lambda c: bk.wait_read(dve, "unet_nat", c), True)
            for q in range(4):
                bk.wait_full(dve, "out3", q)
                xc = x_nat[:, 4 * q:4 * q + 4, :].rearrange("p a b -> p (a b)")
                bk.read(V.tensor_tensor(xc, aux("out3", q), xc, ALU.add), "out3", q)

        @block.tensor
        def _(pe):
            T = nc.tensor

            def transposes(stage, q, src, n):
                bk.wait_free(pe, stage, q)
                for i in range(n):
                    ins = T.transpose(aux(stage, q)[:, i * P:(i + 1) * P], src(i), ident[:, :])
                bk.filled(ins, stage, q)

            pe.wait_ge(sem("consts"), 5)
            pe.wait_ge(sem("ones"), 2)
            pe.wait_ge(sem("vec_in"), 80)
            T.transpose(aux("setup")[:, 0:128], sagew[:, 0:128], ident[:, :])
            T.transpose(aux("setup")[:, 128:256], sagew[:, 128:256], ident[:, :])
            bk.filled(T.transpose(aux("setup")[:, 256:280], vec_rows, ident[0:24, 0:24]), "setup")
            pe.wait_ge(sem("pool_sq"), 1)
            bk.filled(T.matmul(aux("pnorm")[:, 0:3], ones[:, :], degs[:, 0, 0:3], start=True, stop=True), "pnorm")

            for it in range(16):
                a = ring[it % 4]
                ring_row_in(pe, it)
                for q in range(4):
                    u = 4 * it + q
                    bk.wait_free(pe, "adjT", u)
                    for i in range(4):
                        jt = 4 * q + i
                        if jt == it:
                            pe.wait_ge(sem("dblk"), it + 1)
                            src = dblk[:, it % 2, :]
                        else:
                            src = a[:, jt * P:(jt + 1) * P]
                        ins = T.transpose(aux("adjT", u)[:, i * P:(i + 1) * P], src, ident[:, :])
                    bk.filled(ins, "adjT", u)
                    if q == 0:
                        pe.wait_ge(*at("ln_h", 0, it + 1))
                    ins = T.matmul(ps[:, q, :], h_nat[:, it, :], a[:, q * 512:(q + 1) * 512],
                                   start=(it == 0), stop=(it == 15), skip_group_check=True)
                    if it == 15:
                        bk.filled(ins, "msg", q)
                if it < 15:
                    ins.then_inc(sem("row_used_pe"), 1)
            pe.wait_ge(sem("colacc"), 16)
            bk.wait_free(pe, "csum")
            for jt in range(16):
                ins = T.matmul(aux("csum")[:, jt:jt + 1], colacc[:, jt * P:(jt + 1) * P], ones[:, 0:1],
                               start=True, stop=True)
            bk.filled(ins, "csum")

            def to_natural(stage, ready, src, l):
                for q in range(QL[l]):
                    ready(q)
                    transposes(stage, q, lambda i: src[:, (4 * q + i) * P:(4 * q + i + 1) * P],
                               len(chunk_tiles(l, q)))

            def h_transposed(s):
                for q in range(4):
                    pe.wait_ge(*at("ln_h", s, 4 * q + 4))
                    transposes(f"hT{s}", q, lambda i: h_nat[:, 4 * q + i, :], 4)

            def product(stage, ready, correction, passes):
                for q in range(4):
                    bk.wait_free(pe, stage, q)

                def step(k, pairs, start=False, stop=False):
                    for n, (j, xx) in enumerate(pairs):
                        for q in range(4):
                            ins = T.matmul(ps[:, q, :], xx[:, k, :], atp[j][:, k, q * 512:(q + 1) * 512],
                                           start=start and n == 0, stop=stop and n == len(pairs) - 1,
                                           skip_group_check=True)
                            if stop and n == len(pairs) - 1:
                                bk.filled(ins, stage, q)

                for s, (wait, pairs) in enumerate(passes):
                    wait()
                    last = s == len(passes) - 1
                    for c in range(4):
                        if s == 0:
                            ready(c)
                        a, b = 4 * c, 4 * c + 4
                        if s == 0 and c == 0:
                            step(0, pairs, start=True)
                            a = 1
                        if last and c == 3:
                            b = 15
                        with pe.Fori(a, b) as k:
                            step(k, pairs)
                    if last:
                        for k in range(16):
                            for xx in (xh, xl):
                                T.matmul(ps[:, k // 4, blk(k)], xx[:, k, :], correction[:, :],
                                         start=False, stop=False, skip_group_check=True)
                        step(15, pairs, stop=True)

            both = [(0, xh), (0, xl), (1, xh)]

            def x_ready(s):
                def wait(c):
                    pe.wait_ge(*at("x_hi", s, c + 1))
                    pe.wait_ge(*at("x_lo", s, c + 1))
                return wait

            to_natural("msg_nat", lambda q: bk.wait_read(pe, "msg", q), zT0, 0)
            h_transposed(1)
            for q in range(4):
                bk.wait_read(pe, "adjT", 60 + q)
            pe.wait_ge(sem("at_hi"), 64)
            product("prod1", x_ready(1), minus_s, [(lambda: None, both)])

            def dense_out(s, w1, w2, bias):
                for q in range(4):
                    bk.wait_read(pe, f"hT{s}", q)
                    bk.wait_read(pe, f"prod{s}", q)
                    bk.wait_free(pe, f"out{s}", q)
                    for t in range(4 * q, 4 * q + 4):
                        o, c = aux(f"out{s}", q)[:, blk(t)], slice(t * P, (t + 1) * P)
                        T.matmul(o, hT[:, c], w1, start=True, stop=False)
                        ins = T.matmul(o, zT0[:, c], w2, start=False, stop=bias is None)
                        if bias is not None:
                            ins = T.matmul(o, ones[0:1, :], bias, start=False, stop=True)
                    bk.filled(ins, f"out{s}", q)

            def repeat_dn(l, stage):
                for q in range(QL[l]):
                    pe.wait_ge(*at("dn_blocks", stage, chunk_tiles(l, q)[-1] + 1))
                    bk.wait_free(pe, stage, q)
                    bk.filled(T.matmul(aux(stage, q)[:, 0:CW[l]], ones[:, :],
                                       diag[:, 0:len(chunk_tiles(l, q)), :].rearrange("p a b -> p (a b)"),
                                       start=True, stop=True), stage, q)

            pe.wait_ge(sem("sagewT"), 1)
            pe.wait_ge(sem("w_in"), 32)
            dense_out(1, sagewT[:, 0:128], sagewT[:, 128:256], sageb)
            repeat_dn(0, "dnrow0")
            h_transposed(2)

            def conv(g, ready, passes=None):
                l, w = GL[g], CW[GL[g]]
                for q in range(QL[l]):
                    ready(q)
                    bk.wait_free(pe, f"y{g}", q)
                    for t in chunk_tiles(l, q):
                        ins = T.matmul(aux(f"y{g}", q)[:, blk(t)], xin_of(g)[:, t * P:(t + 1) * P], cw[:, g, :],
                                       start=True, stop=True)
                    bk.filled(ins, f"y{g}", q)
                if l == 0:
                    product(f"conv{g}", lambda c: bk.wait_read(pe, f"y{g}", c), plus_s,
                            passes or [(lambda: None, both)])
                    return
                for q in range(QL[l]):
                    bk.wait_free(pe, f"conv{g}", q)
                for k in range(TL[l]):
                    if k % 4 == 0:
                        bk.wait_read(pe, f"y{g}", k // 4)
                    if k == TL[l] - 1:
                        for kk in range(TL[l]):
                            T.matmul(ps[:, kk // 4, blk(kk)], ys[:, kk, :], ident[:, :], start=False, stop=False,
                                     skip_group_check=True)
                    for q in range(QL[l]):
                        ins = T.matmul(ps[:, q, 0:w], ys[:, k, :], aT[l][:, k, q * w:(q + 1) * w],
                                       start=(k == 0), stop=(k == TL[l] - 1), skip_group_check=True)
                        if k == TL[l] - 1:
                            bk.filled(ins, f"conv{g}", q)

            def pooling(l):
                srow, cmp, _, xs = scratch(l)
                w = CW[l]
                pe.wait_ge(*at("pool_b", l, 1))
                for q in range(QL[l]):
                    pe.wait_ge(*at("bn", l, q + 1))
                    bk.wait_free(pe, f"score{l}", q)
                    bk.filled(T.matmul(ps[:, q, 0:w], pool_b, res[l][:, q * w:(q + 1) * w], start=True, stop=True),
                              f"score{l}", q)
                pe.wait_ge(*at("srow", l, 1))
                bk.wait_free(pe, f"scol{l}")
                for t in range(TL[l]):
                    ins = T.transpose(aux(f"scol{l}")[:, t:t + 1], srow[0:1, t * P:(t + 1) * P], ident[0:1, 0:1])
                bk.filled(ins, f"scol{l}")
                to_natural(f"pay{l}", lambda q: None, res[l], l)
                bk.wait_free(pe, f"rank{l}")
                for t in range(TL[l]):
                    pe.wait_ge(*at("cmp", l, cmps(l, t)))
                    for u in range(TL[l]):
                        ins = T.matmul(aux(f"rank{l}")[:, u:u + 1], cmp[t % 2][:, u * P:(u + 1) * P], ones_bf[:, :],
                                       start=(t == 0 and u == 0), stop=(t == TL[l] - 1 and u == TL[l] - 1),
                                       skip_group_check=True)
                    if t < TL[l] - 1:
                        ins.then_inc(sem("cmp_used"), 1)
                bk.filled(ins, f"rank{l}")
                pe.wait_ge(*at("xs_in", l, 16))
                for q in range(QL[l + 1]):
                    transposes(f"xs{l}", q, lambda i: xs[:, 4 * q + i, 0:P], len(chunk_tiles(l + 1, q)))

            conv(0, lambda q: bk.wait_read(pe, "hT2", q))
            pooling(0)

            def sel_l0(rt):
                pe.wait_ge(sem("g_unit"), rt + 1)
                for q in range(4):
                    transposes(f"selL0_{rt}", q, lambda i: g_ring[rt % 3][:, (4 * q + i) * P:(4 * q + i + 1) * P], 4)

            def sel_b0(c):
                pe.wait_ge(sem(f"b_in{c % 2}"), 32 * (c // 2 + 1))
                for q in range(4):
                    bk.wait_free(pe, f"selB0_{c}", q)
                    o = aux(f"selB0_{c}", q).bitcast(F16)
                    for i in range(8):
                        k = 8 * (q % 2) + i
                        ins = T.transpose(o[:, i * P:(i + 1) * P], b_ring[c % 2][q // 2][:, k * P:(k + 1) * P],
                                          ident16[:, :])
                    bk.filled(ins, f"selB0_{c}", q)

            def sel_product(c, halves):
                for q in range(4):
                    bk.wait_read(pe, f"selB0_{c}", q)
                for half in halves:
                    bk.wait_free(pe, f"sel0_{c}_{half}")

                def step(k, start=False, stop=False):
                    for n, (jb, jl) in enumerate(((0, 0), (0, 1), (1, 0))):
                        for half in halves:
                            ins = T.matmul(ps[:, bk.bank(f"sel0_{c}_{half}"), :], sel_b[c % 3][jb][:, k, :],
                                           sel_l[jl][:, k, half * 512:(half + 1) * 512],
                                           start=start and n == 0, stop=stop and n == 2, skip_group_check=True)
                            if stop and n == 2:
                                bk.filled(ins, f"sel0_{c}_{half}")

                step(0, start=True)
                with pe.Fori(1, 15) as k:
                    step(k)
                step(15, stop=True)

            for rt in range(4):
                sel_l0(rt)
            sel_b0(0)
            for rt in range(4):
                for q in range(4):
                    bk.wait_read(pe, f"selL0_{rt}", q)
            sel_product(0, [0])
            for rt in range(4, 8):
                sel_l0(rt)
            sel_b0(1)
            for rt in range(4, 8):
                for q in range(4):
                    bk.wait_read(pe, f"selL0_{rt}", q)
            sel_product(0, [1])
            for c in range(1, 8):
                if c < 7:
                    sel_b0(c + 1)
                sel_product(c, [0, 1])

            for l in (1, 2, 3):
                for c in range(TL[l]):
                    pe.wait_ge(*at("unit", l, c + 1))
                    sel_read(pe, l, c)
                for rt in range(TL[l]):
                    for q in range(QL[l]):
                        transposes(f"nat{l}_{rt}", q, lambda i: aT[l][:, 4 * q + i, rt * P:(rt + 1) * P],
                                   len(chunk_tiles(l, q)))
                repeat_dn(l, f"dnrow{l}")
                conv(l, lambda q: bk.wait_read(pe, f"xs{l - 1}", q))
                if l == 3:
                    break
                pooling(l)
                rsel, csel = lsel(l)
                for rt in range(TL[l + 1]):
                    pe.wait_ge(*at(f"gs_in_{rt % 2}", l, 16 * (rt // 2 + 1)))
                    for q in range(QL[l]):
                        transposes(f"selL{l}_{rt}", q, lambda i: gst[rt % 2][:, (4 * q + i) * P:(4 * q + i + 1) * P],
                                   len(chunk_tiles(l, q)))
                    pe.wait_ge(*at(f"bs_in_{rt % 2}", l, 16 * (rt // 2 + 1)))
                    for q in range(QL[l]):
                        transposes(f"selB{l}_{rt}", q, lambda i: bst[rt % 2][:, (4 * q + i) * P:(4 * q + i + 1) * P],
                                   len(chunk_tiles(l, q)))
                for rt in range(TL[l + 1]):
                    for q in range(QL[l]):
                        bk.wait_read(pe, f"selL{l}_{rt}", q)
                        bk.wait_read(pe, f"selB{l}_{rt}", q)
                for c in range(TL[l + 1]):
                    bk.wait_free(pe, f"sel{l}_{c}")
                    for k in range(TL[l]):
                        ins = T.matmul(ps[:, c % 4, 0:NL[l + 1]], csel[:, k, c * P:(c + 1) * P], rsel[:, k, :],
                                       start=(k == 0), stop=(k == TL[l] - 1))
                    bk.filled(ins, f"sel{l}_{c}")

            for g, l in ((3, 2), (4, 1), (5, 0)):
                to_natural(f"upnat{l}", lambda q: pe.wait_ge(*at("bn", g, q + 1)), bn_out(g), l + 1)
                pe.wait_ge(*at("up_in", l, 16 * TL[l]))
                un = h_nat if l == 0 else upn
                for q in range(QL[l]):
                    transposes(f"upin{l}", q, lambda i: un[:, 4 * q + i, :], len(chunk_tiles(l, q)))
                if l == 0:
                    repeat_dn(0, "dnrow0b")
                    conv(6, lambda q: bk.wait_read(pe, "upin0", q),
                         [(lambda: pe.wait_ge(sem("at_hi_back"), 64), both[:2]),
                          (lambda: pe.wait_ge(sem("at_lo_back"), 64), both[2:])])
                else:
                    conv(g + 1, lambda q: bk.wait_read(pe, f"upin{l}", q))
            to_natural("unet_nat", lambda q: pe.wait_ge(*at("bn", 6, q + 1)), zT0, 0)
            h_transposed(3)
            product("prod3", x_ready(3), minus_s, [(lambda: None, both)])
            pe.wait_ge(sem("catw_in"), 16)
            dense_out(3, catw[:, 0, :], catw[:, 1, :], None)


_INS = ["x", "adj", "L1_gnn_W", "L1_gnn_b", "L2_gnn_conv_w", "L2_gnn_conv_b", "L2_gnn_pool_w",
        "L2_gnn_bn_g", "L2_gnn_bn_b", "L3_gnn_weight"]


def kernel(**inputs):
    import numpy as _np
    import concourse.bacc as _bacc
    from concourse import mybir as _mybir
    from concourse.bass_utils import run_bass_kernel_spmd as _run

    nc = _bacc.Bacc("TRN2", target_bir_lowering=False, num_devices=1)
    arrays, args = {}, []
    for name in _INS:
        a = _np.ascontiguousarray(inputs[name])
        arrays[f"in_{name}"] = a
        args.append(nc.dram_tensor(f"in_{name}", a.shape, _mybir.dt.from_np(a.dtype), kind="ExternalInput").ap())
    args.append(nc.dram_tensor("out", (N0, P), F32, kind="ExternalOutput").ap())
    graph_stack_kernel(nc, *args)
    r = _run(nc, [arrays], core_ids=[0])
    return r.results[0]["out"]
```
